# Optimizing a Trainium2 kernel written in Bass

```python
import numpy as np
import jax
import jax.numpy as jnp

def _softmax(x, axis=-1):
    return jax.nn.softmax(x, axis=axis)

def _gelu(x):
    return jax.nn.gelu(x, approximate=True)

def _silu(x):
    return jax.nn.silu(x)

def _sigmoid(x):
    return jax.nn.sigmoid(x)

def _layernorm(x, axis=-1, eps=1e-05):
    m = jnp.mean(x, axis=axis, keepdims=True)
    v = jnp.var(x, axis=axis, keepdims=True)
    return (x - m) / jnp.sqrt(v + eps)

def _scatter_add(tgt, idx, src, axis=0):
    return tgt.at[idx].add(src)

def _segment_sum(src, seg, n):
    return jax.ops.segment_sum(src, seg, n)
kernel_name = 'mk_adj_ffn_d1_adj_r2_6849b8'

def setup_inputs(seed: int=0):
    np.random.seed(seed)
    _w = jnp.asarray

    def _rec_inputs():
        import jax
        import jax.numpy as jnp
        _gk = jax.random.key(seed)
        x = -0.0002928 + 1 * jax.random.normal(jax.random.fold_in(_gk, 1), (8, 1024, 128), jnp.float32)
        _a = jax.random.bernoulli(jax.random.fold_in(_gk, 2), 0.0078125, (1024, 1024))
        _a = jnp.logical_or(_a, jnp.swapaxes(_a, -1, -2))
        _a = jnp.logical_or(_a, jnp.eye(1024, dtype=bool))
        adj = _a.astype(jnp.int32)
        return (x, adj)
    x, adj = _rec_inputs()

    def _L0_gnn_setup():
        import jax, jax.numpy as jnp
        import numpy as np
        ALPHA = 0.2
        key = jax.random.key(seed)
        k1, k2, k3, k4 = jax.random.split(key, 4)
        B, N, Din, Dout = (8, 1024, 128, 128)
        h = jax.random.normal(k1, (B, N, Din), dtype=jnp.float32)
        adj = jax.random.randint(k2, (N, N), 0, 2, dtype=jnp.int32)
        w_bound = float(np.sqrt(6.0 / (Din + Dout)))
        a_bound = float(np.sqrt(6.0 / (2 * Dout + 1)))
        W = jax.random.uniform(k3, (Din, Dout), dtype=jnp.float32, minval=-w_bound, maxval=w_bound)
        a = jax.random.uniform(k4, (2 * Dout, 1), dtype=jnp.float32, minval=-a_bound, maxval=a_bound)
        return {'h': h, 'adj': adj, 'W': W, 'a': a}
    _L0_gnn_all = _L0_gnn_setup()
    _L0_gnn_in = {k: v for k, v in _L0_gnn_all.items() if k in ('W', 'a')}
    del _L0_gnn_all

    def _L0_ffn_setup():
        import jax, jax.numpy as jnp
        import numpy as np
        DIM = 128
        HEADS = 8
        NUM_KEYS = 128
        NUM_KV = NUM_KEYS ** 2
        PK_TOPK = 16
        FINAL_TOPK = 16
        DIM_KEY = DIM // 2
        P = 2

        def _pk(x, Wq_pk, pk_keys):
            b, n, _ = x.shape
            q = (x @ Wq_pk).reshape(b, n, P, HEADS, DIM_KEY).transpose(2, 0, 1, 3, 4)
            sim = jnp.einsum('pbnhd,pkhd->pbnhk', q, pk_keys)
            scores, idx = jax.lax.top_k(sim, PK_TOPK)
            idx0 = idx[0]
            idx1 = idx[1] * NUM_KEYS
            index = (idx0[..., :, None] + idx1[..., None, :]).reshape(b, n, HEADS, PK_TOPK * PK_TOPK)
            score = (scores[0][..., :, None] + scores[1][..., None, :]).reshape(b, n, HEADS, PK_TOPK * PK_TOPK)
            final_scores, pk_idx = jax.lax.top_k(score, FINAL_TOPK)
            final_indices = jnp.take_along_axis(index, pk_idx, axis=-1)
            final_scores = jax.nn.softmax(final_scores, axis=-1)
            return (final_scores, final_indices)
        key = jax.random.key(seed)
        ks = jax.random.split(key, 7)
        b, n = (2, 512)
        std = 0.02
        x = jax.random.normal(ks[0], (b, n, DIM), dtype=jnp.float32)
        Wq_pk = jax.random.normal(ks[1], (DIM, P * HEADS * DIM_KEY), dtype=jnp.float32) * std
        pk_keys = jax.random.normal(ks[2], (P, NUM_KEYS, HEADS, DIM_KEY), dtype=jnp.float32) * std
        Wq = jax.random.normal(ks[3], (DIM, HEADS * DIM), dtype=jnp.float32) * std
        keys_table = jax.random.normal(ks[4], (NUM_KV * HEADS, DIM), dtype=jnp.float32) * std
        values_table = jax.random.normal(ks[5], (NUM_KV * HEADS, DIM), dtype=jnp.float32) * std
        Wo = jax.random.normal(ks[6], (DIM * HEADS, DIM), dtype=jnp.float32) * std
        return {'x': x, 'Wq_pk': Wq_pk, 'pk_keys': pk_keys, 'Wq': Wq, 'keys_table': keys_table, 'values_table': values_table, 'Wo': Wo}
    _L0_ffn_all = _L0_ffn_setup()
    _L0_ffn_in = {k: v for k, v in _L0_ffn_all.items() if k in ('Wq_pk', 'pk_keys', 'Wq', 'keys_table', 'values_table', 'Wo')}
    del _L0_ffn_all
    return {'x': x, 'adj': adj, 'L0_gnn_W': _L0_gnn_in['W'], 'L0_gnn_a': _L0_gnn_in['a'], 'L0_ffn_Wq_pk': _L0_ffn_in['Wq_pk'], 'L0_ffn_pk_keys': _L0_ffn_in['pk_keys'], 'L0_ffn_Wq': _L0_ffn_in['Wq'], 'L0_ffn_keys_table': _L0_ffn_in['keys_table'], 'L0_ffn_values_table': _L0_ffn_in['values_table'], 'L0_ffn_Wo': _L0_ffn_in['Wo']}

def reference(x, adj, L0_gnn_W, L0_gnn_a, L0_ffn_Wq_pk, L0_ffn_pk_keys, L0_ffn_Wq, L0_ffn_keys_table, L0_ffn_values_table, L0_ffn_Wo):
    import jax
    import jax.numpy as jnp

    def _L0_gnn_ref(h, adj, W, a):
        import jax, jax.numpy as jnp
        import numpy as np
        ALPHA = 0.2
        Wh = jnp.matmul(h, W)
        D = W.shape[1]
        e_src = jnp.matmul(Wh, a[:D])
        e_dst = jnp.matmul(Wh, a[D:])
        e = e_src + jnp.swapaxes(e_dst, 1, 2)
        e = jnp.where(e > 0, e, ALPHA * e)
        mask = (adj > 0)[None, :, :]
        e = jnp.where(mask, e, -jnp.inf)
        alpha_w = jax.nn.softmax(e, axis=-1)
        h_prime = jnp.matmul(alpha_w, Wh)
        return jax.nn.elu(h_prime)

    def _L0_ffn_ref(x, Wq_pk, pk_keys, Wq, keys_table, values_table, Wo):
        import jax, jax.numpy as jnp
        import numpy as np
        DIM = 128
        HEADS = 8
        NUM_KEYS = 128
        NUM_KV = NUM_KEYS ** 2
        PK_TOPK = 16
        FINAL_TOPK = 16
        DIM_KEY = DIM // 2
        P = 2

        def _pk(x, Wq_pk, pk_keys):
            b, n, _ = x.shape
            q = (x @ Wq_pk).reshape(b, n, P, HEADS, DIM_KEY).transpose(2, 0, 1, 3, 4)
            sim = jnp.einsum('pbnhd,pkhd->pbnhk', q, pk_keys)
            scores, idx = jax.lax.top_k(sim, PK_TOPK)
            idx0 = idx[0]
            idx1 = idx[1] * NUM_KEYS
            index = (idx0[..., :, None] + idx1[..., None, :]).reshape(b, n, HEADS, PK_TOPK * PK_TOPK)
            score = (scores[0][..., :, None] + scores[1][..., None, :]).reshape(b, n, HEADS, PK_TOPK * PK_TOPK)
            final_scores, pk_idx = jax.lax.top_k(score, FINAL_TOPK)
            final_indices = jnp.take_along_axis(index, pk_idx, axis=-1)
            final_scores = jax.nn.softmax(final_scores, axis=-1)
            return (final_scores, final_indices)
        b, n, d = x.shape
        q = (x @ Wq).reshape(b, n, HEADS, DIM) * DIM ** (-0.5)
        kv_scores, indices = _pk(x, Wq_pk, pk_keys)
        offsets = jnp.arange(HEADS, dtype=indices.dtype) * NUM_KV
        ind = indices + offsets[None, None, :, None]
        k = jnp.einsum('bnhk,bnhkd->bnhd', kv_scores, keys_table[ind])
        v = jnp.einsum('bnhk,bnhkd->bnhd', kv_scores, values_table[ind])
        sim = jnp.einsum('bihd,bjhd->bhij', q, k)
        neg = -jnp.finfo(sim.dtype).max
        causal = jnp.tril(jnp.ones((n, n), dtype=bool))
        sim = jnp.where(causal, sim, neg)
        attn = jax.nn.softmax(sim, axis=-1)
        out = jnp.einsum('bhij,bjhd->bhid', attn, v)
        out = out.transpose(0, 2, 1, 3).reshape(b, n, HEADS * DIM)
        return out @ Wo
    x = x + _L0_gnn_ref(_layernorm(x, axis=-1), adj, L0_gnn_W, L0_gnn_a)
    x = x + _L0_ffn_ref(_layernorm(x, axis=-1), L0_ffn_Wq_pk, L0_ffn_pk_keys, L0_ffn_Wq, L0_ffn_keys_table, L0_ffn_values_table, L0_ffn_Wo)
    return x

_drawn_inputs = setup_inputs


def setup_inputs(seed=0):
    import zlib

    import numpy as np

    out = dict(_drawn_inputs(seed))
    spreads = {}
    factors = {'L0_ffn_Wq_pk': 8.0,
     'L0_ffn_pk_keys': 8.0,
     'L0_ffn_Wq': 64.0,
     'L0_ffn_keys_table': 64.0,
     'L0_ffn_values_table': 8.0,
     'L0_ffn_Wo': 8.0}
    for name, (base, spread) in spreads.items():
        noise = np.random.default_rng([zlib.crc32(name.encode()), seed]).standard_normal(out[name].shape)
        drawn = base * np.exp(spread * noise) if base else spread * noise
        out[name] = jnp.asarray(drawn.astype(out[name].dtype))
    for name, factor in factors.items():
        out[name] = (out[name] * factor).astype(out[name].dtype)
    return out
```

```python
from contextlib import ExitStack

import concourse.bass as bass
from concourse import mybir

ALU = mybir.AluOpType
ACT = mybir.ActivationFunctionType
F32 = mybir.dt.float32
BF16 = mybir.dt.bfloat16
I32 = mybir.dt.int32
U32 = mybir.dt.uint32
AX_X = mybir.AxisListType.X

P = 128
BATCH = 8
N = 1024
TILES = N // P
HEADS = 8
DK = 64
TOPK = 16
NUM_KV = P * P
KV = 2 * P
RING = 4
UNITS = TILES
PE_ROWS = 8
EPS = 1e-5
ALPHA = 0.2
LEAD = 2
SUMMED = UNITS - LEAD
BIG = 1e30
TAKEN = -3e38
STAIRS = [(0, 1, 16), (1, 1, 8), (2, 2, 5), (4, 4, 3), (8, 8, 1)]
CAND = sum(i * j for _, i, j in STAIRS)


def gat_and_product_key_attention(nc, x, adj, W, WT, a, WqpkT, keysT, Wq, table, Wo, out):
    with ExitStack() as ctx:
        def sb(name, shape, dt=F32):
            return ctx.enter_context(nc.sbuf_tensor(name, shape, dt))

        def bank(name, shape):
            return ctx.enter_context(nc.psum_tensor(name, shape, F32))

        def sem(name):
            return ctx.enter_context(nc.semaphore(name))

        ident = sb("ident", [P, P])
        causal = sb("causal", [P, P])
        rank_u = sb("rank_u", [P, CAND, TOPK], U32)
        rank = sb("rank", [P, CAND, TOPK], BF16)
        head_row = sb("head_row", [P, HEADS])
        mask = sb("mask", [P, TILES, N])
        w_ext = sb("w_ext", [P, P + 1])
        w_t = sb("w_t", [P, P])
        a_sb = sb("a_sb", [P, 2])
        a_ext = sb("a_ext", [P, P + 1])
        w_dst = sb("w_dst", [P, P])
        pk = sb("pk", [P, HEADS, 2, P])
        wq = sb("wq", [P, HEADS, P])
        wo = sb("wo", [P, HEADS, P])
        wq_cur = sb("wq_cur", [P, P])
        xin = sb("xin", [P, TILES, P])
        hn = sb("hn", [P, N])
        hnT = sb("hnT", [P, N])
        wh = sb("wh", [P, TILES, P + 1])
        dst = sb("dst", [P, N])
        edge = sb("edge", [P, N])
        row = sb("row", [P, 16])
        stat = sb("stat", [P, TILES, 6])
        mv = sb("mv", [P, TILES, 2])
        rstd = sb("rstd", [P, TILES])
        hp = sb("hp", [P, P])
        hneg = sb("hneg", [P, P])
        x1 = sb("x1", [P, P])
        xn = sb("xn", [P, P])
        gstat = sb("gstat", [P, 6])
        gmv = sb("gmv", [P, 2])
        acc = sb("acc", [P, 2, TILES * P])
        xnT = sb("xnT", [P, 2, TILES * P])
        xt = sb("xt", [P, 2, P])
        side = sb("side", [P, 2, 2, TOPK])
        sidx = sb("sidx", [P, 2, TOPK], U32)
        left = sb("left", [P, 2, P])
        cand = sb("cand", [P, 2, CAND])
        cleft = sb("cleft", [P, CAND])
        top = sb("top", [P, TOPK])
        ntop = sb("ntop", [P, 1])
        pos = sb("pos", [P, TOPK], U32)
        posb = sb("posb", [P, TOPK], BF16)
        is_at = sb("is_at", [P, CAND, TOPK], BF16)
        hot = sb("hot", [P, CAND, TOPK])
        ew = sb("ew", [P, TOPK])
        ewsum = sb("ewsum", [P, 2])
        wgt = sb("wgt", [P, UNITS, TOPK])
        idx = sb("idx", [P, UNITS, TOPK], U32)
        ring = sb("ring", [P, RING, TOPK, KV])
        part = sb("part", [P, KV])
        kv = sb("kv", [P, TILES, KV])
        diag = sb("diag", [P, PE_ROWS, P])
        kT = sb("kT", [P, TILES * P])
        qT = sb("qT", [P, TILES * P])
        prob = sb("prob", [P, N])
        probT = sb("probT", [P, N])
        oT = sb("oT", [P, P])
        nmax = sb("nmax", [P, 1])
        psum_row = sb("psum_row", [P, 1])
        rz = sb("rz", [P, 1])

        R_MAX, R_M0, R_NM, R_SUM, R_RECIP, R_STD, R_RSTD = range(7)

        ps_v = bank("ps_v", [P, 2, KV])
        ps_t = bank("ps_t", [P, 3, P])
        ps_w = bank("ps_w", [P, 4 * P])
        ps_s = bank("ps_s", [P, N])
        ps_p = bank("ps_p", [P, 2, 4 * P])
        ps_o = bank("ps_o", [P, 2, P])
        pw_ps = ps_w[:, 0:KV]
        wh_ps = ps_w[:, KV:KV + P + 1]
        ps_sim = ps_v[:, 0, :]
        ps_part = ps_v[:, 1, :]
        oT_ps = ps_o[:, 0, :]
        y_ps = ps_o[:, 1, :]

        w_dma = sem("w_dma")
        in_dma = sem("in_dma")
        adj_dma = sem("adj_dma")
        x_dma = sem("x_dma")
        out_dma = sem("out_dma")
        rows_dma = [sem(f"rows_dma{t}") for t in range(UNITS)]
        consts = sem("consts")
        dve_step = sem("dve_step")
        a_ready = sem("a_ready")
        pk_mm = sem("pk_mm")
        pk_copied = sem("pk_copied")
        aux_mm = sem("aux_mm")
        aux_copied = sem("aux_copied")
        hvar = sem("hvar")
        hstd = sem("hstd")
        hn_ready = sem("hn_ready")
        hn_tp = sem("hn_tp")
        hnT_copied = sem("hnT_copied")
        wh_mm = sem("wh_mm")
        wh_copied = sem("wh_copied")
        dst_mm = sem("dst_mm")
        dst_copied = sem("dst_copied")
        g_edge = sem("g_edge")
        g_exp = sem("g_exp")
        g_tp = sem("g_tp")
        g_tp_copied = sem("g_tp_copied")
        g_mm = sem("g_mm")
        g_neg = sem("g_neg")
        g_elu = sem("g_elu")
        g_var = sem("g_var")
        g_std = sem("g_std")
        g_xn = sem("g_xn")
        g_xnT = sem("g_xnT")
        g_xnT_copied = sem("g_xnT_copied")
        xt_copied = sem("xt_copied")
        sim_mm = sem("sim_mm")
        sim_read = sem("sim_read")
        wq_copied = sem("wq_copied")
        q_mm = sem("q_mm")
        q_copied = sem("q_copied")
        top_ready = sem("top_ready")
        exp_top = sem("exp_top")
        idx_ready = sem("idx_ready")
        rows_summed = sem("rows_summed")
        diag_ready = sem("diag_ready")
        pw_mm = sem("pw_mm")
        k_tp = sem("k_tp")
        k_copied = sem("k_copied")
        s_mm = sem("s_mm")
        max_ready = sem("max_ready")
        p_exp = sem("p_exp")
        p_tp = sem("p_tp")
        p_copied = sem("p_copied")
        o_mm = sem("o_mm")
        o_copied = sem("o_copied")
        y_mm = sem("y_mm")
        y_added = sem("y_added")
        sp_mark = sem("sp_mark")
        pool_mark = sem("pool_mark")
        act_mark = sem("act_mark")
        dve_mark = sem("dve_mark")

        HALVES = [1 + (t >= 4) for t in range(TILES)]
        HALVES_ALL = sum(HALVES)

        def halves(n, t):
            return n * HALVES_ALL + sum(HALVES[:t])

        wpk_t = ring[0:DK, 0, :, :].rearrange("p a b -> p (a b)")[:, 0:2 * HEADS * P] \
            .rearrange("p (m n) -> p m n", n=P)
        keys_t = ring[0:DK, 1, :, :].rearrange("p a b -> p (a b)")[:, 0:2 * HEADS * P] \
            .rearrange("p (m n) -> p m n", n=P)

        block = ctx.enter_context(nc.Block())


        @block.sync
        def _(sp):
            sp.dma_start(xin[:], x[0].rearrange("(t p) d -> p t d", p=P)).then_inc(x_dma, 16)
            sp.dma_start(w_t[:], WT).then_inc(w_dma, 16)
            sp.dma_start(a_sb[:], a).then_inc(w_dma, 16)
            sp.dma_start(w_ext[:, 0:P], W).then_inc(w_dma, 16)
            sp.dma_start(mask[:].bitcast(I32), adj.rearrange("(t p) n -> p t n", p=P)).then_inc(adj_dma, 16)
            sp.dma_start(wpk_t, WqpkT).then_inc(in_dma, 16)
            sp.dma_start(keys_t, keysT).then_inc(in_dma, 16)
            sp.dma_start(wq[:], Wq.rearrange("p (h n) -> p h n", h=HEADS)).then_inc(in_dma, 16)
            sp.dma_start(wo[:], Wo.rearrange("(h p) n -> p h n", p=P)).then_inc(in_dma, 16)

            def stores(b):
                for t in range(TILES):
                    sp.wait_ge(y_added, b * HEADS * UNITS + (HEADS - 1) * UNITS + t + 1)
                    sp.sem_inc(sp_mark, 1)
                    src = acc[:, bass.ds(b % 2, 1), t * P:(t + 1) * P].rearrange("p o n -> p (o n)")
                    dst_ = out[bass.ds(b, 1), t * P:(t + 1) * P, :].rearrange("o p n -> (o p) n")
                    sp.dma_start(dst_, src).then_inc(out_dma, 16)

            def load(b):
                sp.wait_ge(g_xn, b * TILES)
                sp.sem_inc(sp_mark, 1)
                sp.dma_start(xin[:], x[bass.ds(b, 1)].rearrange("o (t p) d -> (o p) t d", p=P)) \
                    .then_inc(x_dma, 16)

            load(1)
            with sp.Fori(2, BATCH) as b:
                load(b)
                stores(b - 2)
            stores(BATCH - 2)
            stores(BATCH - 1)
            sp.wait_ge(out_dma, BATCH * TILES * 16)

        @block.gpsimd
        def _(pool):
            nc.gpsimd.memset(ident[:], 0.0).then_inc(consts, 1)
            nc.gpsimd.memset(causal[:], 0.0).then_inc(consts, 1)
            nc.gpsimd.iota(rank_u[:], pattern=[[1, CAND], [0, TOPK]], base=0, channel_multiplier=0).then_inc(consts, 1)
            for h in range(HEADS):
                nc.gpsimd.memset(head_row[:, h:h + 1], float(h * NUM_KV)).then_inc(consts, 1)
            pool.wait_ge(consts, 3 + HEADS)
            nc.gpsimd.affine_select(out=ident[:], in_=ident[:], compare_op=ALU.not_equal, fill=1.0,
                                    base=0, pattern=[[-1, P]], channel_multiplier=1).then_inc(consts, 1)
            nc.gpsimd.affine_select(out=causal[:], in_=causal[:], compare_op=ALU.is_ge, fill=-BIG,
                                    base=0, pattern=[[-1, P]], channel_multiplier=1).then_inc(consts, 1)

            def gathers(t):
                for k in range(TOPK):
                    pool.indirect_dma_start(
                        out=ring[:, t % RING, k, :], out_offset=None, in_=table,
                        in_offset=bass.IndirectOffsetOnAxis(ap=idx[:, t, k:k + 1], axis=0),
                        bounds_check=HEADS * NUM_KV - 1, oob_is_err=True).then_inc(rows_dma[t], 16)

            for t in range(UNITS):
                pool.wait_ge(idx_ready, t + 1)
                if t == 0:
                    pool.wait_ge(pk_mm, 4)
                if t >= RING:
                    pool.wait_ge(rows_summed, t - RING + 1)
                gathers(t)
            with pool.Fori(1, BATCH * HEADS) as n:
                for t in range(UNITS):
                    pool.wait_ge(idx_ready, n * UNITS + t + 1)
                    pool.wait_ge(rows_summed, n * UNITS + t - RING + 1)
                    pool.sem_inc(pool_mark, 1)
                    gathers(t)

        @block.scalar
        def _(act):
            def projection(bn):
                act.wait_ge(hvar, bn + 1)
                nc.scalar.activation(rstd[:], mv[:, :, 1], ACT.Sqrt).then_inc(hstd, 1)
                for c in range(2):
                    act.wait_ge(hn_tp, 2 * bn + c + 1)
                    nc.scalar.copy(hnT[:, c * 512:(c + 1) * 512], ps_p[:, c, :]).then_inc(hnT_copied, 1)
                for t in range(TILES):
                    act.wait_ge(wh_mm, TILES * bn + t + 1)
                    nc.scalar.copy(wh[:, t, :], ps_p[:, t % 2, 0:P + 1]).then_inc(wh_copied, 1)
                for c in range(2):
                    act.wait_ge(dst_mm, 2 * bn + c + 1)
                    nc.scalar.copy(dst[:, c * 512:(c + 1) * 512], ps_p[:, c, :]).then_inc(dst_copied, 1)

            def graph_exp(g):
                act.wait_ge(g_edge, g + 1)
                nc.scalar.activation(hn[:], edge[:], ACT.Exp, bias=row[:, R_NM:R_NM + 1],
                                     accum_out=row[:, R_SUM:R_SUM + 1]).then_inc(g_exp, 1)

            def graph_copy(g):
                for c in range(2):
                    act.wait_ge(g_tp, 2 * g + c + 1)
                    nc.scalar.copy(hnT[:, c * 512:(c + 1) * 512], ps_p[:, c, :]).then_inc(g_tp_copied, 1)

            def graph_elu(g):
                act.wait_ge(g_neg, g + 1)
                nc.scalar.activation(hneg[:], hneg[:], ACT.Exp).then_inc(g_elu, 1)

            def graph_sqrt(g):
                act.wait_ge(g_var, g + 1)
                nc.scalar.activation(row[:, R_STD:R_STD + 1], row[:, R_STD:R_STD + 1], ACT.Sqrt).then_inc(g_std, 1)

            def graph_keep(bn, it, g):
                act.wait_ge(g_xnT, g + 1)
                act.sem_inc(act_mark, 1)
                nc.scalar.copy(xnT[:, bass.ds(bn % 2, 1), bass.ds(it * P, P)].rearrange("p o n -> p (o n)"),
                               ps_t[:, 1, :]).then_inc(g_xnT_copied, 1)

            def choose_begin(b, a_unit, t):
                if not isinstance(a_unit, int) or a_unit >= 2:
                    act.wait_ge(q_mm, a_unit - 1)
                act.wait_ge(g_xnT_copied, b * TILES + t + 1)
                act.sem_inc(act_mark, 1)
                nc.scalar.copy(xt[:, t % 2, :],
                               xnT[:, bass.ds(b % 2, 1), t * P:(t + 1) * P].rearrange("p o n -> p (o n)")) \
                    .then_inc(xt_copied, 1)

            def choose_query(a_unit, t):
                act.wait_ge(q_mm, a_unit + 1)
                nc.scalar.mul(qT[:, t * P:(t + 1) * P], ps_t[:, 2, :], float(P) ** -0.5).then_inc(q_copied, 1)

            def choose_softmax(a_unit):
                act.wait_ge(top_ready, a_unit + 1)
                nc.scalar.activation(ew[:], top[:], ACT.Exp, bias=ntop[:, 0:1],
                                     accum_out=ewsum[:, 0:1]).then_inc(exp_top, 1)

            def query_weights(h, heads_done):
                act.wait_ge(q_mm, heads_done * UNITS)
                act.sem_inc(act_mark, 1)
                nc.scalar.copy(wq_cur[:], wq[:, bass.ds(h, 1), :].rearrange("p o n -> p (o n)")) \
                    .then_inc(wq_copied, 1)

            def diagonals(n, t):
                act.wait_ge(pw_mm, n * UNITS + t)
                act.wait_ge(idx_ready, n * UNITS + t + 1)
                for k in range(PE_ROWS):
                    nc.scalar.mul(diag[:, k, :], ident[:], wgt[:, t, k:k + 1]).then_inc(diag_ready, 1)

            def attend_begin(n, t):
                act.wait_ge(k_tp, n * UNITS + t + 1)
                nc.scalar.copy(kT[:, t * P:(t + 1) * P], ps_t[:, 0, :]).then_inc(k_copied, 1)

            def attend(n, t):
                cols = (t + 1) * P
                act.wait_ge(max_ready, n * UNITS + t + 1)
                nc.scalar.activation(prob[:, 0:cols], ps_s[:, 0:cols], ACT.Exp, bias=nmax[:, 0:1],
                                     accum_out=psum_row[:, 0:1]).then_inc(p_exp, 1)
                for c in range(HALVES[t]):
                    m = min(512, cols - 512 * c)
                    act.wait_ge(p_tp, halves(n, t) + c + 1)
                    nc.scalar.copy(probT[:, c * 512:c * 512 + m], ps_p[:, c, 0:m]).then_inc(p_copied, 1)
                act.wait_ge(o_mm, n * UNITS + t + 1)
                nc.scalar.copy(oT[:], oT_ps).then_inc(o_copied, 1)

            act.wait_ge(aux_mm, 1)
            nc.scalar.copy(w_ext[:, P:P + 1], wh_ps[:, 0:1]).then_inc(aux_copied, 1)
            nc.scalar.copy(w_dst[:], wh_ps[:, 1:P + 1]).then_inc(aux_copied, 1)
            projection(0)
            for g in range(4):
                act.wait_ge(pk_mm, g + 1)
                nc.scalar.copy(pk[:].rearrange("p h s n -> p (h s n)")[:, g * 512:(g + 1) * 512],
                               ps_s[:, g % 2 * 512:(g % 2 + 1) * 512]).then_inc(pk_copied, 1)
            act.wait_ge(in_dma, 4 * 16)
            nc.scalar.copy(wq_cur[:], wq[:, 0, :]).then_inc(wq_copied, 1)
            graph_exp(0)
            graph_copy(0)
            for it in range(TILES):
                if it >= LEAD:
                    diagonals(0, it - LEAD)
                graph_elu(it)
                graph_sqrt(it)
                graph_keep(0, it, it)
                choose_begin(0, it, it)
                choose_query(it, it)
                if it < TILES - 1:
                    graph_exp(it + 1)
                    graph_copy(it + 1)
                choose_softmax(it)
            choose_begin(0, UNITS, 0)
            diagonals(0, SUMMED)
            query_weights(1, 1)

            def head(b, h, n, graph, ahead, first=False):
                if ahead and not first:
                    query_weights((h + 1) % HEADS, n + 1)
                for t in range(UNITS):
                    if graph:
                        g = n + TILES
                        if t == 1:
                            graph_exp(g)
                        if t == 2:
                            graph_copy(g)
                        if t == 4:
                            graph_elu(g)
                        if t == 5:
                            graph_sqrt(g)
                        if t == 6:
                            graph_keep(b + 1, h, g)
                    if t:
                        attend(n, t - 1)
                    elif not first:
                        attend(n - 1, UNITS - 1)
                    if ahead:
                        t1 = (t + 1) % UNITS
                        n1 = n + 1 + (t + 1) // UNITS
                        choose_begin(n1 // HEADS if graph else BATCH - 1, n1 * UNITS + t1, t1)
                        choose_softmax((n + 1) * UNITS + t)
                    attend_begin(n, t)
                    if t < UNITS - 1:
                        if not first or t + 1 > SUMMED:
                            diagonals(n, t + 1)
                    elif ahead:
                        diagonals(n + 1, 0)
                    if ahead:
                        choose_query((n + 1) * UNITS + t, t)
                if not ahead:
                    attend(n, UNITS - 1)

            projection(1)
            head(0, 0, 0, True, True, True)
            with act.Fori(1, HEADS) as h:
                head(0, h, h, True, True)
            with act.Fori(1, BATCH - 1) as b:
                projection(b + 1)
                with act.Fori(0, HEADS) as h:
                    head(b, h, b * HEADS + h, True, True)
            last = BATCH - 1
            with act.Fori(0, HEADS - 1) as h:
                head(last, h, last * HEADS + h, False, True)
            head(last, HEADS - 1, BATCH * HEADS - 1, False, False)

        @block.tensor
        def _(pe):
            def projection(bn):
                if not isinstance(bn, int):
                    pe.wait_ge(p_copied, halves((bn - 1) * HEADS, 0) - HALVES[-1])
                elif bn:
                    pe.wait_ge(g_tp_copied, 2 * TILES)
                for c in range(2):
                    pe.wait_ge(hn_ready, TILES * bn + 4 * c + 4)
                    for j in range(4):
                        t = 4 * c + j
                        ins = nc.tensor.transpose(ps_p[:, c, j * P:(j + 1) * P], hn[:, t * P:(t + 1) * P], ident[:])
                    ins.then_inc(hn_tp, 1)
                pe.wait_ge(hnT_copied, 2 * bn + 2)
                if isinstance(bn, int) and bn == 0:
                    pe.wait_ge(aux_copied, 2)
                for t in range(TILES):
                    if t >= 2:
                        pe.wait_ge(wh_copied, TILES * bn + t - 1)
                    nc.tensor.matmul(ps_p[:, t % 2, 0:P + 1], hnT[:, t * P:(t + 1) * P], w_ext[:],
                                     start=True, stop=True).then_inc(wh_mm, 1)
                pe.wait_ge(wh_copied, TILES * (bn + 1))
                for c in range(2):
                    nc.tensor.matmul(ps_p[:, c, :], w_dst[:], hnT[:, c * 512:(c + 1) * 512],
                                     start=True, stop=True).then_inc(dst_mm, 1)

            def graph_transposes(g):
                pe.wait_ge(g_exp, g + 1)
                for c in range(2):
                    for j in range(4):
                        t = 4 * c + j
                        ins = nc.tensor.transpose(ps_p[:, c, j * P:(j + 1) * P], hn[:, t * P:(t + 1) * P], ident[:])
                    ins.then_inc(g_tp, 1)

            def graph_sum(bn, g, place):
                pe.wait_ge(wh_copied, TILES * (bn + 1))
                pe.wait_ge(g_neg, g)
                pe.wait_ge(g_tp_copied, 2 * g + 2)
                for j in range(TILES):
                    ins = nc.tensor.matmul(place[:, 0:P], hnT[:, j * P:(j + 1) * P], wh[:, j, 0:P],
                                           start=(j == 0), stop=(j == TILES - 1))
                ins.then_inc(g_mm, 1)

            def graph_turn(g, queries):
                pe.wait_ge(g_xn, g + 1)
                pe.wait_ge(g_xnT_copied, g)
                pe.wait_ge(q_copied, queries)
                nc.tensor.transpose(ps_t[:, 1, :], xn[:], ident[:]).then_inc(g_xnT, 1)

            def similarities(h, a_unit, t):
                pe.wait_ge(xt_copied, a_unit + 1)
                pe.wait_ge(sim_read, a_unit)
                if isinstance(a_unit, int) and a_unit == 0:
                    pe.wait_ge(pk_copied, 4)
                nc.tensor.matmul(ps_sim, xt[:, t % 2, :],
                                 pk[:, bass.ds(h, 1), :, :].rearrange("p o s n -> p (o s n)"),
                                 start=True, stop=True).then_inc(sim_mm, 1)

            def query(a_unit, t, weights):
                pe.wait_ge(q_copied, a_unit)
                pe.wait_ge(wq_copied, weights)
                nc.tensor.matmul(ps_t[:, 2, :], wq_cur[:], xt[:, t % 2, :], start=True, stop=True) \
                    .then_inc(q_mm, 1)

            def weigh(n, t, graph):
                u = n * UNITS + t
                pe.wait_ge(rows_dma[t], (n + 1) * TOPK * 16)
                pe.wait_ge(diag_ready, (u + 1) * PE_ROWS)
                pe.wait_ge(rows_summed, u)
                if t == 4 and graph:
                    pe.wait_ge(g_neg, n + TILES + 1)
                for k in range(PE_ROWS):
                    ins = nc.tensor.matmul(pw_ps, diag[:, k, :], ring[:, t % RING, k, :],
                                           start=(k == 0), stop=(k == PE_ROWS - 1))
                ins.then_inc(pw_mm, 1)

            def turn_keys(n, t, queries, rows):
                u = n * UNITS + t
                pe.wait_ge(rows_summed, u + 1)
                pe.wait_ge(q_copied, queries)
                if t == 6:
                    pe.wait_ge(g_xnT_copied, rows)
                nc.tensor.transpose(ps_t[:, 0, :], kv[:, t, 0:P], ident[:]).then_inc(k_tp, 1)

            def scores(n, t):
                u = n * UNITS + t
                if isinstance(n, int) and u == 0:
                    pe.wait_ge(g_neg, TILES)
                pe.wait_ge(k_copied, u + 1)
                pe.wait_ge(p_exp, u)
                q = qT[:, t * P:(t + 1) * P]
                cols = (t + 1) * P
                for c in range(HALVES[t]):
                    m = min(512, cols - 512 * c)
                    nc.tensor.matmul(ps_s[:, c * 512:c * 512 + m], q, kT[:, c * 512:c * 512 + m],
                                     start=True, stop=(c < HALVES[t] - 1))
                nc.tensor.matmul(ps_s[:, t * P:cols], ident[:], causal[:], start=False, stop=True) \
                    .then_inc(s_mm, 1)

            def attend(h, n, t, graph, projected, rows):
                u = n * UNITS + t
                first_unit = isinstance(u, int) and u == 0
                pe.wait_ge(p_exp, u + 1)
                pe.wait_ge(p_copied, halves(n, t))
                if t == 1 and graph:
                    pe.wait_ge(g_tp_copied, rows * 2)
                if t == UNITS - 1 or first_unit:
                    pe.wait_ge(dst_copied, projected * 2)
                for c in range(HALVES[t]):
                    for j in range(4 * c, min(4 * c + 4, t + 1)):
                        ins = nc.tensor.transpose(ps_p[:, c, (j % 4) * P:(j % 4 + 1) * P],
                                                  prob[:, j * P:(j + 1) * P], ident[:])
                    ins.then_inc(p_tp, 1)
                pe.wait_ge(y_added, u)
                pe.wait_ge(p_copied, halves(n, t) + HALVES[t])
                for j in range(t + 1):
                    ins = nc.tensor.matmul(oT_ps, kv[:, j, P:KV], probT[:, j * P:(j + 1) * P],
                                           start=(j == 0), stop=(j == t))
                ins.then_inc(o_mm, 1)
                pe.wait_ge(o_copied, u + 1)
                nc.tensor.matmul(y_ps, oT[:], wo[:, bass.ds(h, 1), :].rearrange("p o n -> p (o n)"),
                                 start=True, stop=True).then_inc(y_mm, 1)

            pe.wait_ge(w_dma, 3 * 16)
            pe.wait_ge(a_ready, 2)
            nc.tensor.matmul(wh_ps, w_t[:], a_ext[:], start=True, stop=True).then_inc(aux_mm, 1)
            pe.wait_ge(consts, 5 + HEADS)
            projection(0)
            pe.wait_ge(in_dma, 4 * 16)
            for g in range(4):
                if g >= 2:
                    pe.wait_ge(pk_copied, g - 1)
                for j in range(4):
                    m = 4 * g + j
                    ins = nc.tensor.matmul(ps_s[:, (4 * (g % 2) + j) * P:(4 * (g % 2) + j + 1) * P],
                                           wpk_t[:, m, :], keys_t[:, m, :], start=True, stop=True)
                ins.then_inc(pk_mm, 1)
            pe.wait_ge(dst_copied, 2)
            graph_transposes(0)
            graph_sum(0, 0, ps_s)
            for it in range(TILES):
                graph_turn(it, it)
                similarities(0, it, it)
                query(it, it, 1)
                if it >= LEAD:
                    weigh(0, it - LEAD, False)
                if it < TILES - 1:
                    graph_transposes(it + 1)
                    graph_sum(0, it + 1, ps_s)
            pe.wait_ge(rows_summed, SUMMED)
            similarities(1, UNITS, 0)

            def head(b, h, n, graph, ahead, first=False):
                projected = b + 2 if graph else BATCH
                rows = n + TILES + 1 if graph else BATCH * TILES
                for t in range(UNITS):
                    if graph and t == 3:
                        pe.wait_ge(rows_summed, n * UNITS + t)
                        graph_sum(b + 1, n + TILES, wh_ps)
                    if not first or t >= SUMMED:
                        weigh(n, t, graph)
                    if graph:
                        if t == 2:
                            pe.wait_ge(p_copied, halves(n, 1))
                            graph_transposes(n + TILES)
                        if t == 6:
                            graph_turn(n + TILES, (n + 1) * UNITS + t)
                    if t:
                        attend(h, n, t - 1, graph, projected, rows)
                    elif not first:
                        attend((h + HEADS - 1) % HEADS, n - 1, UNITS - 1, graph, projected, rows)
                    turn_keys(n, t, (n + 1) * UNITS + (t if ahead else 0), rows)
                    if ahead:
                        t1 = (t + 1) % UNITS
                        n1 = n + 1 + (t + 1) // UNITS
                        similarities(n1 % HEADS, n1 * UNITS + t1, t1)
                    scores(n, t)
                    if ahead:
                        query((n + 1) * UNITS + t, t, n + 2)
                if not ahead:
                    attend(h, n, UNITS - 1, graph, projected, rows)

            projection(1)
            head(0, 0, 0, True, True, True)
            with pe.Fori(1, HEADS) as h:
                head(0, h, h, True, True)
            with pe.Fori(1, BATCH - 1) as b:
                projection(b + 1)
                with pe.Fori(0, HEADS) as h:
                    head(b, h, b * HEADS + h, True, True)
            last = BATCH - 1
            with pe.Fori(0, HEADS - 1) as h:
                head(last, h, last * HEADS + h, False, True)
            head(last, HEADS - 1, BATCH * HEADS - 1, False, False)

        @block.vector
        def _(dve):
            steps = [0]

            def step(ins):
                steps[0] += 1
                ins.then_inc(dve_step, 1)
                return steps[0]

            def after(count):
                dve.wait_ge(dve_step, count)

            def clear_steps():
                after(steps[0])
                dve.sem_clear(dve_step)
                steps[0] = 0

            def projection(bn):
                dve.wait_ge(x_dma, 16 * (bn + 1))
                for t in range(TILES):
                    c = step(nc.vector.bn_stats(stat[:, t, :], xin[:, t, :]))
                after(c)
                for t in range(TILES):
                    c = step(nc.vector.bn_aggr(mv[:, t, :], stat[:, t, :]))
                after(c)
                nc.vector.tensor_scalar(mv[:, :, 1], mv[:, :, 1], EPS, None, ALU.add).then_inc(hvar, 1)
                dve.wait_ge(hstd, bn + 1)
                c = step(nc.vector.reciprocal(rstd[:], rstd[:]))
                after(c)
                dve.wait_ge(g_mm, TILES * bn)
                for t in range(TILES):
                    nc.vector.tensor_scalar(hn[:, t * P:(t + 1) * P], xin[:, t, :], mv[:, t, 0:1],
                                            rstd[:, t:t + 1], ALU.subtract, ALU.mult).then_inc(hn_ready, 1)

            def graph_edges(bn, it, g):
                src = wh[:, bass.ds(it, 1), P:P + 1].rearrange("p o n -> p (o n)")
                m = mask[:, bass.ds(it, 1), :].rearrange("p o n -> p (o n)")
                dve.wait_ge(dst_copied, 2 * bn + 2)
                dve.wait_ge(g_exp, g)
                c = step(nc.vector.tensor_tensor(edge[:], dst[:], m, ALU.add))
                after(c)
                c = step(nc.vector.tensor_reduce(row[:, R_MAX:R_MAX + 1], edge[:], AX_X, ALU.max))
                c = step(nc.vector.tensor_scalar(edge[:], edge[:], src, None, ALU.add))
                after(c)
                c1 = step(nc.vector.tensor_scalar(row[:, R_M0:R_M0 + 1], row[:, R_MAX:R_MAX + 1], src, None, ALU.add))
                after(c1)
                c1 = step(nc.vector.scalar_tensor_tensor(
                    out=row[:, R_M0:R_M0 + 1], in0=row[:, R_M0:R_M0 + 1], scalar=ALPHA,
                    in1=row[:, R_M0:R_M0 + 1], op0=ALU.mult, op1=ALU.max))
                after(c1)
                c1 = step(nc.vector.tensor_scalar(row[:, R_NM:R_NM + 1], row[:, R_M0:R_M0 + 1], -1.0, None, ALU.mult))
                after(c1)
                nc.vector.scalar_tensor_tensor(out=edge[:], in0=edge[:], scalar=ALPHA, in1=edge[:],
                                               op0=ALU.mult, op1=ALU.max).then_inc(g_edge, 1)

            def graph_elu(it, g, place):
                dve.wait_ge(g_exp, g + 1)
                c = step(nc.vector.reciprocal(row[:, R_RECIP:R_RECIP + 1], row[:, R_SUM:R_SUM + 1]))
                after(c)
                dve.wait_ge(g_mm, g + 1)
                c = step(nc.vector.tensor_scalar(hp[:], place[:, 0:P], row[:, R_RECIP:R_RECIP + 1], None, ALU.mult))
                after(c)
                nc.vector.tensor_scalar(hneg[:], hp[:], 0.0, None, ALU.min).then_inc(g_neg, 1)
                xrow = xin[:, bass.ds(it, 1), :].rearrange("p o n -> p (o n)")
                c = step(nc.vector.scalar_tensor_tensor(out=x1[:], in0=hp[:], scalar=0.0, in1=xrow,
                                                        op0=ALU.max, op1=ALU.add))
                after(c)

            def graph_out(bn, it, g, first):
                dve.wait_ge(g_elu, g + 1)
                c = step(nc.vector.scalar_tensor_tensor(out=x1[:], in0=hneg[:], scalar=-1.0, in1=x1[:],
                                                        op0=ALU.add, op1=ALU.add))
                after(c)
                c = step(nc.vector.bn_stats(gstat[:], x1[:]))
                if not first:
                    dve.wait_ge(out_dma, 16 * TILES * (bn - 1))
                c1 = step(nc.vector.tensor_scalar(
                    acc[:, bass.ds(bn % 2, 1), bass.ds(it * P, P)].rearrange("p o n -> p (o n)"),
                    x1[:], 0.0, None, ALU.add))
                after(c)
                c = step(nc.vector.bn_aggr(gmv[:], gstat[:]))
                after(c)
                nc.vector.tensor_scalar(row[:, R_STD:R_STD + 1], gmv[:, 1:2], EPS, None, ALU.add).then_inc(g_var, 1)

            def graph_norm(g):
                dve.wait_ge(g_std, g + 1)
                c = step(nc.vector.reciprocal(row[:, R_RSTD:R_RSTD + 1], row[:, R_STD:R_STD + 1]))
                after(c)
                dve.wait_ge(g_xnT, g)
                nc.vector.tensor_scalar(xn[:], x1[:], gmv[:, 0:1], row[:, R_RSTD:R_RSTD + 1],
                                        ALU.subtract, ALU.mult).then_inc(g_xn, 1)

            row_sum = [0]

            def add_row(n, t, k):
                w = wgt[:, t, k:k + 1]
                rows = ring[:, t % RING, k, :]
                if k == PE_ROWS:
                    row_sum[0] = step(nc.vector.tensor_scalar(ps_part, rows, w, None, ALU.mult))
                    return
                after(row_sum[0])
                row_sum[0] = step(nc.vector.scalar_tensor_tensor(
                    out=part[:] if k == TOPK - 1 else ps_part, in0=rows, scalar=w, in1=ps_part,
                    op0=ALU.mult, op1=ALU.add))

            def sum_rows(n, t):
                dve.wait_ge(pw_mm, n * UNITS + t + 1)
                if t == 0:
                    dve.wait_ge(o_mm, n * UNITS)
                after(row_sum[0])
                nc.vector.tensor_tensor(kv[:, t, :], part[:], pw_ps, ALU.add).then_inc(rows_summed, 1)

            def no_row(n, t, k):
                pass

            def choose_sets(h, t, a_unit):
                sim = [ps_sim[:, s * P:(s + 1) * P] for s in range(2)]
                dve.wait_ge(sim_mm, a_unit + 1)
                dve.sem_inc(dve_mark, 1)
                m = [step(nc.vector.max(side[:, s, 0, 0:8], sim[s])) for s in range(2)]
                for s in range(2):
                    after(m[s])
                    m[s] = step(nc.vector.match_replace(left[:, s, :], side[:, s, 0, 0:8], sim[s], TAKEN))
                for s in range(2):
                    step(nc.vector.max_index(sidx[:, s, 0:8], side[:, s, 0, 0:8], sim[s]))
                for s in range(2):
                    after(m[s])
                    m[s] = step(nc.vector.max(side[:, s, 0, 8:16], left[:, s, :]))
                for s in range(2):
                    after(m[s])
                    m[s] = step(nc.vector.max_index(sidx[:, s, 8:16], side[:, s, 0, 8:16], left[:, s, :]))
                after(m[0])
                hrow = head_row[:, bass.ds(h, 1)]
                c = step(nc.vector.tensor_scalar(side[:, 0, 1, :], sidx[:, 0, :], hrow, None, ALU.add))
                after(m[1])
                nc.vector.tensor_scalar(side[:, 1, 1, :], sidx[:, 1, :], float(P), None, ALU.mult) \
                    .then_inc(sim_read, 1)
                return c

            def choose_sums(n, t, a_unit, c, add):
                add(n, t, PE_ROWS)
                add(n, t, PE_ROWS + 1)
                dve.wait_ge(sim_read, a_unit + 1)
                after(c)
                at = 0
                for i0, ni, nj in STAIRS:
                    o = cand[:, :, at:at + ni * nj].rearrange("p c (i j) -> p c i j", j=nj)
                    s0 = side[:, 0, :, i0:i0 + ni].unsqueeze(3).broadcast_to([P, 2, ni, nj])
                    s1 = side[:, 1, :, 0:nj].unsqueeze(2).broadcast_to([P, 2, ni, nj])
                    c = step(nc.vector.tensor_tensor(o, s0, s1, ALU.add))
                    at += ni * nj
                add(n, t, PE_ROWS + 2)
                after(c)
                c = step(nc.vector.max(top[:, 0:8], cand[:, 0, :]))
                add(n, t, PE_ROWS + 3)
                after(c)
                c = step(nc.vector.match_replace(cleft[:], top[:, 0:8], cand[:, 0, :], TAKEN))
                step(nc.vector.max_index(pos[:, 0:8], top[:, 0:8], cand[:, 0, :]))
                add(n, t, PE_ROWS + 4)
                after(c)
                c = step(nc.vector.max(top[:, 8:16], cleft[:]))
                add(n, t, PE_ROWS + 5)
                after(c)
                nc.vector.tensor_scalar(ntop[:], top[:, 0:1], -1.0, None, ALU.mult).then_inc(top_ready, 1)
                c = step(nc.vector.max_index(pos[:, 8:16], top[:, 8:16], cleft[:]))
                add(n, t, PE_ROWS + 6)
                after(c)
                c = step(nc.vector.tensor_copy(posb[:], pos[:]))
                add(n, t, PE_ROWS + 7)
                after(c)
                return step(nc.vector.tensor_tensor(
                    is_at[:], rank[:], posb[:].unsqueeze(1).broadcast_to([P, CAND, TOPK]), ALU.is_equal))

            def choose_rows(t, a_unit, c):
                after(c)
                c = step(nc.vector.tensor_tensor(hot[:], is_at[:],
                                                 cand[:, 1, :].unsqueeze(2).broadcast_to([P, CAND, TOPK]), ALU.mult))
                dve.wait_ge(exp_top, a_unit + 1)
                c1 = step(nc.vector.reciprocal(ewsum[:, 1:2], ewsum[:, 0:1]))
                after(c1)
                step(nc.vector.tensor_scalar(wgt[:, t, :], ew[:], ewsum[:, 1:2], None, ALU.mult))
                after(c)
                with nc.allow_low_precision("row numbers, whole and under 2**24"):
                    nc.vector.tensor_reduce(idx[:, t, :], hot[:].rearrange("p c k -> p k c"), AX_X, ALU.add) \
                        .then_inc(idx_ready, 1)

            dve.wait_ge(consts, 5 + HEADS)
            step(nc.vector.tensor_copy(rank[:], rank_u[:]))
            step(nc.vector.memset(row[:], 0.0))
            dve.wait_ge(w_dma, 3 * 16)
            nc.vector.tensor_copy(a_ext[:, 0:1], a_sb[:, 0:1]).then_inc(a_ready, 1)
            nc.vector.tensor_copy(a_ext[:, 1:P + 1], a_sb[:, 1:2].broadcast_to([P, P])).then_inc(a_ready, 1)
            projection(0)
            dve.wait_ge(adj_dma, 16)
            for t in range(TILES):
                c = step(nc.vector.tensor_scalar(mask[:, t, :], mask[:, t, :].bitcast(I32), 0, -BIG,
                                                 ALU.is_le, ALU.mult))
            after(c)
            graph_edges(0, 0, 0)
            for it in range(TILES):
                graph_elu(it, it, ps_s)
                graph_out(0, it, it, True)
                graph_norm(it)
                if it < TILES - 1:
                    graph_edges(0, it + 1, it + 1)
                c = choose_sets(0, it, it)
                if it >= LEAD:
                    dve.wait_ge(rows_dma[it - LEAD], TOPK * 16)
                    c = choose_sums(0, it - LEAD, it, c, add_row)
                    sum_rows(0, it - LEAD)
                else:
                    c = choose_sums(0, it, it, c, no_row)
                choose_rows(it, it, c)
            clear_steps()

            def row_max(n, t):
                dve.wait_ge(s_mm, n * UNITS + t + 1)
                nc.vector.tensor_reduce(nmax[:], ps_s[:, 0:(t + 1) * P], AX_X, ALU.max, negate=True) \
                    .then_inc(max_ready, 1)

            def add_head(b, n, t):
                u = n * UNITS + t
                dve.wait_ge(p_exp, u + 1)
                c = step(nc.vector.reciprocal(rz[:], psum_row[:]))
                after(c)
                dve.wait_ge(y_mm, u + 1)
                place = acc[:, bass.ds(b % 2, 1), t * P:(t + 1) * P].rearrange("p o n -> p (o n)")
                nc.vector.scalar_tensor_tensor(out=place, in0=y_ps, scalar=rz[:, 0:1], in1=place,
                                               op0=ALU.mult, op1=ALU.add).then_inc(y_added, 1)

            def head(b, h, n, graph, ahead, first=False):
                for t in range(UNITS):
                    a_unit = (n + 1) * UNITS + t
                    if ahead:
                        c = choose_sets((h + 1) % HEADS, t, a_unit)
                    if t:
                        row_max(n, t - 1)
                    elif not first:
                        row_max(n - 1, UNITS - 1)
                    dve.wait_ge(rows_dma[t], (n + 1) * TOPK * 16)
                    if first and t < SUMMED:
                        c = choose_sums(n, t, a_unit, c, no_row)
                        choose_rows(t, a_unit, c)
                    elif ahead:
                        c = choose_sums(n, t, a_unit, c, add_row)
                        sum_rows(n, t)
                        choose_rows(t, a_unit, c)
                    else:
                        dve.wait_ge(sim_mm, BATCH * HEADS * UNITS + 1)
                        for k in range(PE_ROWS, TOPK):
                            add_row(n, t, k)
                        sum_rows(n, t)
                    if t:
                        add_head(b, n, t - 1)
                    elif not first:
                        add_head((n - 1) // HEADS, n - 1, UNITS - 1)
                    if graph:
                        g = n + TILES
                        if t == 0:
                            graph_edges(b + 1, h, g)
                        if t == 3:
                            graph_elu(h, g, wh_ps)
                        if t == 4:
                            graph_out(b + 1, h, g, first)
                        if t == 5:
                            graph_norm(g)
                if not ahead:
                    row_max(n, UNITS - 1)
                    add_head(b, n, UNITS - 1)
                clear_steps()

            projection(1)
            head(0, 0, 0, True, True, True)
            with dve.Fori(1, HEADS) as h:
                head(0, h, h, True, True)
            with dve.Fori(1, BATCH - 1) as b:
                projection(b + 1)
                clear_steps()
                with dve.Fori(0, HEADS) as h:
                    head(b, h, b * HEADS + h, True, True)
            last = BATCH - 1
            with dve.Fori(0, HEADS - 1) as h:
                head(last, h, last * HEADS + h, False, True)
            head(last, HEADS - 1, BATCH * HEADS - 1, False, False)


def kernel(x, adj, L0_gnn_W, L0_gnn_a, L0_ffn_Wq_pk, L0_ffn_pk_keys, L0_ffn_Wq, L0_ffn_keys_table,
           L0_ffn_values_table, L0_ffn_Wo):
    import numpy as np
    import concourse.bacc as bacc
    from concourse.bass_utils import run_bass_kernel_spmd

    f = np.asarray
    W = f(L0_gnn_W)
    ins = {
        "x": f(x), "adj": f(adj), "W": W, "WT": W.T, "a": f(L0_gnn_a).reshape(2, P).T,
        "WqpkT": f(L0_ffn_Wq_pk).reshape(P, 2, HEADS, DK).transpose(3, 2, 1, 0).reshape(DK, 2 * HEADS, P),
        "keysT": f(L0_ffn_pk_keys).transpose(3, 2, 0, 1).reshape(DK, 2 * HEADS, P),
        "Wq": f(L0_ffn_Wq),
        "table": np.concatenate([f(L0_ffn_keys_table), f(L0_ffn_values_table)], axis=1),
        "Wo": f(L0_ffn_Wo),
    }
    nc = bacc.Bacc("TRN2", target_bir_lowering=False, num_devices=1)
    arrays, args = {}, []
    for name, v in ins.items():
        v = np.ascontiguousarray(v)
        arrays[f"in_{name}"] = v
        args.append(nc.dram_tensor(f"in_{name}", v.shape, mybir.dt.from_np(v.dtype), kind="ExternalInput").ap())
    args.append(nc.dram_tensor("out_x", (BATCH, N, P), F32, kind="ExternalOutput").ap())
    gat_and_product_key_attention(nc, *args)
    return run_bass_kernel_spmd(nc, [arrays], core_ids=[0]).results[0]["out_x"]
```
